# Optimizing a Trainium2 kernel written in Bass

```python
import numpy as np
import jax
import jax.numpy as jnp

def _softmax(x, axis=-1):
    return jax.nn.softmax(x, axis=axis)

def _gelu(x):
    return jax.nn.gelu(x, approximate=True)

def _silu(x):
    return jax.nn.silu(x)

def _sigmoid(x):
    return jax.nn.sigmoid(x)

def _layernorm(x, axis=-1, eps=1e-05):
    m = jnp.mean(x, axis=axis, keepdims=True)
    v = jnp.var(x, axis=axis, keepdims=True)
    return (x - m) / jnp.sqrt(v + eps)

def _scatter_add(tgt, idx, src, axis=0):
    return tgt.at[idx].add(src)

def _segment_sum(src, seg, n):
    return jax.ops.segment_sum(src, seg, n)
kernel_name = 'mk_decoder_postln_d1_seqx_r4_7f85cb'

def setup_inputs(seed: int=0):
    np.random.seed(seed)
    _w = jnp.asarray

    def _rec_inputs():
        import jax
        import jax.numpy as jnp
        _rk = jax.random.key(seed)
        x = -0.0005146 + 1 * jax.random.normal(jax.random.fold_in(_rk, 1), (4, 512, 256), jnp.float32)
        _lenS = 512 - jax.random.randint(jax.random.fold_in(_rk, 7), (4,), 0, max(1, 512 // 4) + 1, jnp.int32)
        _lenS2 = 1601 - jax.random.randint(jax.random.fold_in(_rk, 8), (4,), 0, max(1, 1601 // 4) + 1, jnp.int32)
        _ctx_1024P = jax.random.normal(jax.random.fold_in(_rk, 11), (4, 16, 256), jnp.float32)
        _ctx_1024c = jax.random.dirichlet(jax.random.fold_in(_rk, 511), 0.3 * jnp.ones((16,), jnp.float32), (4, 1601))
        _ctx_1024t = jnp.einsum('bsk,bkd->bsd', _ctx_1024c, _ctx_1024P)
        _ctx_1024t = _ctx_1024t * jax.lax.rsqrt(jnp.mean(jnp.square(_ctx_1024t)) + 1e-12) * 0.953939
        ctx_1024 = -0.000125008 + 0.999885 * (_ctx_1024t + 0.3 * jax.random.normal(jax.random.fold_in(_rk, 611), (4, 1601, 256), jnp.float32))
        return (x, ctx_1024)
    x, ctx_1024 = _rec_inputs()

    def _L0_attn_setup():
        import math
        import jax, jax.numpy as jnp
        import numpy as np
        D_MODEL = 256
        D_STATE = 16
        D_CONV = 4
        EXPAND = 2
        D_INNER = EXPAND * D_MODEL
        DT_RANK = math.ceil(D_MODEL / 16)
        BATCH, SEQ = (1, 512)
        DT_MIN, DT_MAX, DT_FLOOR = (0.001, 0.1, 0.0001)

        def _mamba(x, W_in, conv_w, conv_b, W_x, W_dt, b_dt, A_log, D, W_out):
            B, L, _ = x.shape
            xz = x @ W_in.T
            xs, z = jnp.split(xz, 2, axis=-1)
            xc = jnp.pad(xs.transpose(0, 2, 1), ((0, 0), (0, 0), (D_CONV - 1, 0)))
            xc = jax.lax.conv_general_dilated(xc, conv_w, (1,), 'VALID', dimension_numbers=('NCH', 'OIH', 'NCH'), feature_group_count=D_INNER)
            xs = jax.nn.silu(xc.transpose(0, 2, 1) + conv_b[None, None, :])
            A = -jnp.exp(A_log)
            x_dbl = xs @ W_x.T
            dt, Bm, Cm = jnp.split(x_dbl, [DT_RANK, DT_RANK + D_STATE], axis=-1)
            dt = jax.nn.softplus(dt @ W_dt.T + b_dt)
            dA = jnp.exp(dt[..., None] * A)
            dBx = dt[..., None] * Bm[:, :, None, :] * xs[..., None]

            def step(h, inputs):
                dA_t, dBx_t, C_t = inputs
                h = dA_t * h + dBx_t
                y = jnp.einsum('bdn,bn->bd', h, C_t)
                return (h, y)
            h0 = jnp.zeros((B, D_INNER, D_STATE), xs.dtype)
            _, ys = jax.lax.scan(step, h0, (dA.transpose(1, 0, 2, 3), dBx.transpose(1, 0, 2, 3), Cm.transpose(1, 0, 2)))
            y = ys.transpose(1, 0, 2) + xs * D
            return y * jax.nn.silu(z) @ W_out.T
        key = jax.random.key(seed)
        ks = jax.random.split(key, 8)
        x = jax.random.normal(ks[0], (BATCH, SEQ, D_MODEL), jnp.float32)
        W_in = jax.random.normal(ks[1], (2 * D_INNER, D_MODEL), jnp.float32) / np.sqrt(D_MODEL)
        conv_w = jax.random.normal(ks[2], (D_INNER, 1, D_CONV), jnp.float32) / np.sqrt(D_CONV)
        conv_b = jnp.zeros((D_INNER,), jnp.float32)
        W_x = jax.random.normal(ks[3], (DT_RANK + 2 * D_STATE, D_INNER), jnp.float32) / np.sqrt(D_INNER)
        dt_std = DT_RANK ** (-0.5)
        W_dt = jax.random.uniform(ks[4], (D_INNER, DT_RANK), jnp.float32, -dt_std, dt_std)
        dt = jnp.exp(jax.random.uniform(ks[5], (D_INNER,), jnp.float32) * (math.log(DT_MAX) - math.log(DT_MIN)) + math.log(DT_MIN))
        dt = jnp.clip(dt, DT_FLOOR, None)
        b_dt = dt + jnp.log(-jnp.expm1(-dt))
        A_log = jnp.log(jnp.tile(jnp.arange(1, D_STATE + 1, dtype=jnp.float32), (D_INNER, 1)))
        D = jnp.ones((D_INNER,), jnp.float32)
        W_out = jax.random.normal(ks[6], (D_MODEL, D_INNER), jnp.float32) / np.sqrt(D_INNER)
        return {'x': x, 'W_in': W_in, 'conv_w': conv_w, 'conv_b': conv_b, 'W_x': W_x, 'W_dt': W_dt, 'b_dt': b_dt, 'A_log': A_log, 'D': D, 'W_out': W_out}
    _L0_attn_all = _L0_attn_setup()
    _L0_attn_in = {k: v for k, v in _L0_attn_all.items() if k in ('W_in', 'conv_w', 'conv_b', 'W_x', 'W_dt', 'b_dt', 'A_log', 'D', 'W_out')}
    del _L0_attn_all

    def _L0_xattn_setup():
        import jax, jax.numpy as jnp
        import numpy as np
        DIM = 256
        HEADS = 16
        DIM_HEAD = 64
        INNER = HEADS * DIM_HEAD
        EPS = 1e-05

        def layer_norm(x, gamma, beta):
            mu = jnp.mean(x, axis=-1, keepdims=True)
            var = jnp.mean(jnp.square(x - mu), axis=-1, keepdims=True)
            return (x - mu) * jax.lax.rsqrt(var + EPS) * gamma + beta
        key = jax.random.key(seed)
        ks = jax.random.split(key, 6)
        b, n1, n2 = (8, 1024, 64)
        x = jax.random.normal(ks[0], (b, n1, DIM), dtype=jnp.float32)
        latents = jax.random.normal(ks[1], (b, n2, DIM), dtype=jnp.float32)
        s = 1.0 / np.sqrt(DIM)
        Wq = jax.random.normal(ks[2], (DIM, INNER), dtype=jnp.float32) * s
        Wkv = jax.random.normal(ks[3], (DIM, 2 * INNER), dtype=jnp.float32) * s
        Wout = jax.random.normal(ks[4], (INNER, DIM), dtype=jnp.float32) * (1.0 / np.sqrt(INNER))
        g1 = jnp.ones((DIM,), jnp.float32)
        b1 = jnp.zeros((DIM,), jnp.float32)
        g2 = jnp.ones((DIM,), jnp.float32)
        b2 = jnp.zeros((DIM,), jnp.float32)
        return {'x': x, 'latents': latents, 'g1': g1, 'b1': b1, 'g2': g2, 'b2': b2, 'Wq': Wq, 'Wkv': Wkv, 'Wout': Wout}
    _L0_xattn_all = _L0_xattn_setup()
    _L0_xattn_in = {k: v for k, v in _L0_xattn_all.items() if k in ('g1', 'b1', 'g2', 'b2', 'Wq', 'Wkv', 'Wout')}
    del _L0_xattn_all

    def _L0_ffn_setup():
        import jax, jax.numpy as jnp
        import numpy as np
        B, S, DIM = (2, 512, 256)
        HID = 512
        E, NSH, TOPK = (8, 2, 2)

        def _ffn(x, w1, w2, w3):
            return jax.nn.silu(x @ w1.T) * (x @ w3.T) @ w2.T
        key = jax.random.key(seed)
        ks = jax.random.split(key, 8)
        sc = 0.02
        return {'x': jax.random.normal(ks[0], (B, S, DIM), jnp.float32), 'router_w': jax.random.normal(ks[1], (E, DIM), jnp.float32) * sc, 'expert_bias': jnp.zeros((E,), jnp.float32), 'w1': jax.random.normal(ks[2], (E, HID, DIM), jnp.float32) * sc, 'w3': jax.random.normal(ks[3], (E, HID, DIM), jnp.float32) * sc, 'w2': jax.random.normal(ks[4], (E, DIM, HID), jnp.float32) * sc, 'sw1': jax.random.normal(ks[5], (NSH, HID, DIM), jnp.float32) * sc, 'sw3': jax.random.normal(ks[6], (NSH, HID, DIM), jnp.float32) * sc, 'sw2': jax.random.normal(ks[7], (NSH, DIM, HID), jnp.float32) * sc}
    _L0_ffn_all = _L0_ffn_setup()
    _L0_ffn_in = {k: v for k, v in _L0_ffn_all.items() if k in ('router_w', 'expert_bias', 'w1', 'w3', 'w2', 'sw1', 'sw3', 'sw2')}
    del _L0_ffn_all
    return {'x': x, 'ctx_1024': ctx_1024, 'L0_attn_W_in': _L0_attn_in['W_in'], 'L0_attn_conv_w': _L0_attn_in['conv_w'], 'L0_attn_conv_b': _L0_attn_in['conv_b'], 'L0_attn_W_x': _L0_attn_in['W_x'], 'L0_attn_W_dt': _L0_attn_in['W_dt'], 'L0_attn_b_dt': _L0_attn_in['b_dt'], 'L0_attn_A_log': _L0_attn_in['A_log'], 'L0_attn_D': _L0_attn_in['D'], 'L0_attn_W_out': _L0_attn_in['W_out'], 'L0_xattn_g1': _L0_xattn_in['g1'], 'L0_xattn_b1': _L0_xattn_in['b1'], 'L0_xattn_g2': _L0_xattn_in['g2'], 'L0_xattn_b2': _L0_xattn_in['b2'], 'L0_xattn_Wq': _L0_xattn_in['Wq'], 'L0_xattn_Wkv': _L0_xattn_in['Wkv'], 'L0_xattn_Wout': _L0_xattn_in['Wout'], 'L0_ffn_router_w': _L0_ffn_in['router_w'], 'L0_ffn_expert_bias': _L0_ffn_in['expert_bias'], 'L0_ffn_w1': _L0_ffn_in['w1'], 'L0_ffn_w3': _L0_ffn_in['w3'], 'L0_ffn_w2': _L0_ffn_in['w2'], 'L0_ffn_sw1': _L0_ffn_in['sw1'], 'L0_ffn_sw3': _L0_ffn_in['sw3'], 'L0_ffn_sw2': _L0_ffn_in['sw2']}

def reference(x, ctx_1024, L0_attn_W_in, L0_attn_conv_w, L0_attn_conv_b, L0_attn_W_x, L0_attn_W_dt, L0_attn_b_dt, L0_attn_A_log, L0_attn_D, L0_attn_W_out, L0_xattn_g1, L0_xattn_b1, L0_xattn_g2, L0_xattn_b2, L0_xattn_Wq, L0_xattn_Wkv, L0_xattn_Wout, L0_ffn_router_w, L0_ffn_expert_bias, L0_ffn_w1, L0_ffn_w3, L0_ffn_w2, L0_ffn_sw1, L0_ffn_sw3, L0_ffn_sw2):
    import jax
    import jax.numpy as jnp

    def _L0_attn_ref(x, W_in, conv_w, conv_b, W_x, W_dt, b_dt, A_log, D, W_out):
        import math
        import jax, jax.numpy as jnp
        import numpy as np
        D_MODEL = 256
        D_STATE = 16
        D_CONV = 4
        EXPAND = 2
        D_INNER = EXPAND * D_MODEL
        DT_RANK = math.ceil(D_MODEL / 16)
        BATCH, SEQ = (1, 512)
        DT_MIN, DT_MAX, DT_FLOOR = (0.001, 0.1, 0.0001)

        def _mamba(x, W_in, conv_w, conv_b, W_x, W_dt, b_dt, A_log, D, W_out):
            B, L, _ = x.shape
            xz = x @ W_in.T
            xs, z = jnp.split(xz, 2, axis=-1)
            xc = jnp.pad(xs.transpose(0, 2, 1), ((0, 0), (0, 0), (D_CONV - 1, 0)))
            xc = jax.lax.conv_general_dilated(xc, conv_w, (1,), 'VALID', dimension_numbers=('NCH', 'OIH', 'NCH'), feature_group_count=D_INNER)
            xs = jax.nn.silu(xc.transpose(0, 2, 1) + conv_b[None, None, :])
            A = -jnp.exp(A_log)
            x_dbl = xs @ W_x.T
            dt, Bm, Cm = jnp.split(x_dbl, [DT_RANK, DT_RANK + D_STATE], axis=-1)
            dt = jax.nn.softplus(dt @ W_dt.T + b_dt)
            dA = jnp.exp(dt[..., None] * A)
            dBx = dt[..., None] * Bm[:, :, None, :] * xs[..., None]

            def step(h, inputs):
                dA_t, dBx_t, C_t = inputs
                h = dA_t * h + dBx_t
                y = jnp.einsum('bdn,bn->bd', h, C_t)
                return (h, y)
            h0 = jnp.zeros((B, D_INNER, D_STATE), xs.dtype)
            _, ys = jax.lax.scan(step, h0, (dA.transpose(1, 0, 2, 3), dBx.transpose(1, 0, 2, 3), Cm.transpose(1, 0, 2)))
            y = ys.transpose(1, 0, 2) + xs * D
            return y * jax.nn.silu(z) @ W_out.T
        return _mamba(x, W_in, conv_w, conv_b, W_x, W_dt, b_dt, A_log, D, W_out)

    def _L0_xattn_ref(x, latents, g1, b1, g2, b2, Wq, Wkv, Wout):
        import jax, jax.numpy as jnp
        import numpy as np
        DIM = 256
        HEADS = 16
        DIM_HEAD = 64
        INNER = HEADS * DIM_HEAD
        EPS = 1e-05

        def layer_norm(x, gamma, beta):
            mu = jnp.mean(x, axis=-1, keepdims=True)
            var = jnp.mean(jnp.square(x - mu), axis=-1, keepdims=True)
            return (x - mu) * jax.lax.rsqrt(var + EPS) * gamma + beta
        b, l, _ = latents.shape
        xn = layer_norm(x, g1, b1)
        ln = layer_norm(latents, g2, b2)
        q = ln @ Wq
        kv_input = jnp.concatenate([xn, ln], axis=1)
        kv = kv_input @ Wkv
        k, v = jnp.split(kv, 2, axis=-1)

        def heads(t):
            return t.reshape(t.shape[0], t.shape[1], HEADS, DIM_HEAD).transpose(0, 2, 1, 3)
        q, k, v = (heads(q), heads(k), heads(v))
        scale = 1.0 / np.sqrt(np.sqrt(DIM_HEAD))
        logits = jnp.einsum('bhqd,bhkd->bhqk', q * scale, k * scale)
        w = jax.nn.softmax(logits.astype(jnp.float32), axis=-1).astype(logits.dtype)
        out = jnp.einsum('bhqk,bhkd->bhqd', w, v)
        out = out.transpose(0, 2, 1, 3).reshape(b, l, INNER)
        return out @ Wout

    def _L0_ffn_ref(x, router_w, expert_bias, w1, w3, w2, sw1, sw3, sw2):
        import jax, jax.numpy as jnp
        import numpy as np
        B, S, DIM = (2, 512, 256)
        HID = 512
        E, NSH, TOPK = (8, 2, 2)

        def _ffn(x, w1, w2, w3):
            return jax.nn.silu(x @ w1.T) * (x @ w3.T) @ w2.T
        bs, sl, d = x.shape
        xf = x.reshape(-1, d)
        shared = jnp.zeros_like(xf)
        for i in range(sw1.shape[0]):
            shared = shared + _ffn(xf, sw1[i], sw2[i], sw3[i])
        logits = xf @ router_w.T + expert_bias
        rw, sel = jax.lax.top_k(logits, TOPK)
        rw = jax.nn.softmax(rw.astype(jnp.float32), axis=-1).astype(x.dtype)
        onehot = jax.nn.one_hot(sel, E, dtype=x.dtype)
        combine = jnp.einsum('tk,tke->te', rw, onehot)

        def body(acc, ew):
            e1, e3, e2, cw = ew
            acc = acc + cw[:, None] * _ffn(xf, e1, e2, e3)
            return (acc, None)
        out, _ = jax.lax.scan(body, jnp.zeros_like(xf), (w1, w3, w2, combine.T))
        out = out + shared
        return out.reshape(bs, sl, -1)
    x = _layernorm(x + _L0_attn_ref(x, L0_attn_W_in, L0_attn_conv_w, L0_attn_conv_b, L0_attn_W_x, L0_attn_W_dt, L0_attn_b_dt, L0_attn_A_log, L0_attn_D, L0_attn_W_out), axis=-1)
    x = _layernorm(x + _L0_xattn_ref(ctx_1024, x, L0_xattn_g1, L0_xattn_b1, L0_xattn_g2, L0_xattn_b2, L0_xattn_Wq, L0_xattn_Wkv, L0_xattn_Wout), axis=-1)
    x = _layernorm(x + _L0_ffn_ref(x, L0_ffn_router_w, L0_ffn_expert_bias, L0_ffn_w1, L0_ffn_w3, L0_ffn_w2, L0_ffn_sw1, L0_ffn_sw3, L0_ffn_sw2), axis=-1)
    return x

_drawn_inputs = setup_inputs


def setup_inputs(seed=0):
    import zlib

    import numpy as np

    out = dict(_drawn_inputs(seed))
    spreads = {'L0_attn_conv_b': (0.0, 0.1),
     'L0_attn_D': (1.0, 0.2),
     'L0_xattn_g1': (1.0, 0.2),
     'L0_xattn_b1': (0.0, 0.1),
     'L0_xattn_g2': (1.0, 0.2),
     'L0_xattn_b2': (0.0, 0.1),
     'L0_ffn_expert_bias': (0.0, 0.8)}
    factors = {'L0_attn_W_dt': 2.801,
     'L0_ffn_router_w': 3.897,
     'L0_ffn_w1': 3.359,
     'L0_ffn_w3': 3.322,
     'L0_ffn_w2': 3.325}
    for name, (base, spread) in spreads.items():
        noise = np.random.default_rng([zlib.crc32(name.encode()), seed]).standard_normal(out[name].shape)
        drawn = base * np.exp(spread * noise) if base else spread * noise
        out[name] = jnp.asarray(drawn.astype(out[name].dtype))
    for name, factor in factors.items():
        out[name] = (out[name] * factor).astype(out[name].dtype)
    return out
```

```python
from contextlib import ExitStack

import concourse.bass as bass
from concourse import mybir

F32 = mybir.dt.float32
F32R = mybir.dt.float32r
BF16 = mybir.dt.bfloat16
ALU = mybir.AluOpType
ACT = mybir.ActivationFunctionType
AX_X = mybir.AxisListType.X

P = 128
B, S, DM = 4, 512, 256
TT = S // P
KD = DM // P
EPS = 1e-5

DI, NS, DC, DTR = 512, 16, 4, 16
CT = DI // P


def mamba(nc, x, w_in_t, conv_w, conv_b, w_x_t, w_dt_t, b_dt, a_log, d_skip, w_out_t, x1):
    XD = DTR + 2 * NS
    RING = KD + 2 * CT + 1 + CT + 2 * NS + 2
    AREAD = KD + 2 * CT + CT + NS
    DREAD = 1 + CT + NS + 2
    with ExitStack() as ctx:
        def sb(name, shape, dt=F32):
            return ctx.enter_context(nc.sbuf_tensor(name, shape, dt))

        def sem(name):
            return ctx.enter_context(nc.semaphore(name))

        ring = ctx.enter_context(nc.psum_tensor("m_ring", [P, 4, 512], F32))
        ps_y = ctx.enter_context(nc.psum_tensor("m_y", [P, CT, S], F32))

        win = sb("m_win", [P, KD, 2 * DI])
        wx = sb("m_wx", [P, CT, P])
        wdt = sb("m_wdt", [P, DI])
        wout = sb("m_wout", [P, CT, DM])
        cw = sb("m_cw", [P, CT, DC])
        cb = sb("m_cb", [P, CT])
        bdt = sb("m_bdt", [P, CT])
        a_neg = sb("m_a", [P, CT, NS])
        dsk = sb("m_d", [P, CT])
        ident = sb("m_ident", [P, P])
        diag_d = sb("m_diag", [P, CT, P])
        sel = sb("m_sel", [P, 2 * NS, P], BF16)
        x_in = sb("m_xin", [P, TT, DM])
        x_res = sb("m_xres", [P, TT, DM])
        xt = sb("m_xt", [P, KD, S])
        xs_pad = sb("m_xspad", [P, CT, S + DC - 1])
        zs = sb("m_zs", [P, CT, S])
        cv = sb("m_cv", [P, CT, S])
        xs = sb("m_xs", [P, CT, S])
        xdf = sb("m_xdf", [P, S])
        xdr = sb("m_xdr", [P, S])
        xd3 = sb("m_xd3", [P, 3, S], BF16)
        relu_dt = sb("m_relu", [P, CT, S])
        ew = sb("m_w", [P, CT, S])
        dt = sb("m_dt", [P, CT, S])
        du = sb("m_du", [P, CT, S])
        dA = sb("m_dA", [P, 2, CT, S])
        bsb = sb("m_bsb", [P, 2, S])
        dbx = sb("m_dbx", [P, 2, CT, S])
        h = sb("m_h", [P, 2, CT, S])
        stats = sb("m_stats", [P, TT, 6])
        mv = sb("m_mv", [P, TT, 2])
        rstd = sb("m_rstd", [P, TT])
        half = sb("m_half", [P, TT])

        w_loaded = sem("m_w_loaded")
        a_loaded = sem("m_a_loaded")
        x_loaded = sem("m_x_loaded")
        xres_loaded = sem("m_xres_loaded")
        x_in_free = sem("m_x_in_free")
        consts_set = sem("m_consts_set")
        a_set = sem("m_a_set")
        bank_full = sem("m_bank_full")
        act_read = sem("m_act_read")
        dve_read = sem("m_dve_read")
        dve_step = sem("m_dve_step")
        conv_done = sem("m_conv_done")
        xs_ready = sem("m_xs_ready")
        xd_ready = sem("m_xd_ready")
        exp_done = sem("m_exp_done")
        one_added = sem("m_one_added")
        ln_done = sem("m_ln_done")
        dt_ready = sem("m_dt_ready")
        du_ready = sem("m_du_ready")
        dA_ready = sem("m_dA_ready")
        dbx_ready = sem("m_dbx_ready")
        h_scanned = sem("m_h_scanned")
        y_added = sem("m_y_added")
        g_ready = sem("m_g_ready")
        var_ready = sem("m_var_ready")
        stats_seen = sem("m_stats_seen")
        rstd_ready = sem("m_rstd_ready")

        block = ctx.enter_context(nc.Block())

        @block.sync
        def _(sp):
            sp.dma_start(win[:], w_in_t.rearrange("(k p) n -> p k n", p=P)).then_inc(w_loaded, 16)
            sp.dma_start(cw[:], conv_w).then_inc(w_loaded, 16)
            sp.wait_ge(consts_set, 1)
            sp.dma_start(wx[:, :, 0:XD], w_x_t.rearrange("(c p) n -> p c n", p=P)).then_inc(w_loaded, 16)
            sp.dma_start(wdt[0:DTR, :], w_dt_t).then_inc(w_loaded, 16)
            sp.dma_start(wout[:], w_out_t.rearrange("(c p) n -> p c n", p=P)).then_inc(w_loaded, 16)
            with sp.Fori(0, B) as b:
                sp.wait_ge(x_in_free, b + 1)
                sp.dma_start(x_in[:], x[bass.ds(b, 1)].rearrange("o (t p) d -> p (o t) d", p=P)).then_inc(x_loaded, 16)
                sp.wait_ge(dve_read, b * DREAD + 2)
                sp.dma_start(x_res[:], x[bass.ds(b, 1)].rearrange("o (t p) d -> p (o t) d", p=P)).then_inc(xres_loaded, 16)

        @block.gpsimd
        def _(pool):
            nc.gpsimd.memset(wx[:], 0.0)
            nc.gpsimd.memset(wdt[:], 0.0).then_inc(consts_set, 1)
            nc.gpsimd.memset(ident[:], 0.0)
            nc.gpsimd.memset(sel[:], 0.0)
            nc.gpsimd.memset(half[:], -0.5)
            nc.gpsimd.memset(xs_pad[:], 0.0)
            nc.gpsimd.memset(dA[:, :, :, 0:1], 0.0).then_inc(consts_set, 1)
            pool.wait_ge(consts_set, 2)
            nc.gpsimd.affine_select(out=ident[:], in_=ident[:], compare_op=ALU.not_equal, fill=1.0, base=0,
                                    pattern=[[-1, P]], channel_multiplier=1)
            nc.gpsimd.affine_select(out=sel[:], in_=sel[:], compare_op=ALU.not_equal, fill=1.0, base=-DTR,
                                    pattern=[[-1, 2 * NS], [0, P]], channel_multiplier=1).then_inc(consts_set, 1)

            def times_b(b, n, i):
                pool.wait_ge(act_read, b * AREAD + (KD + 3 * CT + 1) + n)
                pool.wait_ge(h_scanned, b * NS + n + 1)
                nc.gpsimd.tensor_tensor(dbx[:, i], du[:], bsb[:, i:i + 1, :].to_broadcast([P, CT, S]),
                                        ALU.mult).then_inc(dbx_ready, 1)

            pool.sem_inc(dbx_ready, 2)
            with pool.Fori(0, B) as b:
                pool.wait_ge(du_ready, b + 1)
                pool.sem_inc(stats_seen, 1)
                with pool.Fori(0, NS // 2) as pair:
                    times_b(b, 2 * pair, 0)
                    times_b(b, 2 * pair + 1, 1)
                pool.wait_ge(var_ready, b + 1)
                nc.gpsimd.tensor_tensor(rstd[:], mv[:, :, 1], half[:], ALU.pow).then_inc(rstd_ready, 1)

        @block.scalar
        def _(act):
            act.dma_start(a_neg[:], a_log).then_inc(a_loaded, 16)
            for dst, src in ((cb, conv_b), (bdt, b_dt), (dsk, d_skip)):
                act.dma_start(dst[:], src).then_inc(w_loaded, 16)
            act.wait_ge(a_loaded, 16)
            nc.scalar.activation(a_neg[:], a_neg[:], ACT.Exp).then_inc(a_set, 1)
            act.wait_ge(w_loaded, 16 * 8)
            act.wait_ge(consts_set, 3)
            act.wait_ge(a_set, 2)
            with act.Fori(0, B) as b:
                full, seen = b * RING, b * AREAD
                for k in range(KD):
                    act.wait_ge(bank_full, full + k + 1)
                    nc.scalar.activation(xt[:, k], ring[:, k], ACT.Copy).then_inc(act_read, 1)
                for c in range(CT):
                    act.wait_ge(bank_full, full + KD + c + 1)
                    nc.scalar.activation(xs_pad[:, c, DC - 1:], ring[:, (KD + c) % 4], ACT.Copy).then_inc(act_read, 1)
                for c in range(CT):
                    act.wait_ge(bank_full, full + KD + CT + c + 1)
                    nc.scalar.activation(zs[:, c], ring[:, (KD + CT + c) % 4], ACT.Silu).then_inc(act_read, 1)
                for c in range(CT):
                    act.wait_ge(conv_done, b * CT + c + 1)
                    nc.scalar.activation(xs[:, c], cv[:, c], ACT.Silu, bias=cb[:, c:c + 1]).then_inc(xs_ready, 1)
                act.wait_ge(xs_ready, (b + 1) * CT)
                for c in range(CT):
                    act.wait_ge(bank_full, full + KD + 2 * CT + 1 + c + 1)
                    nc.scalar.activation(cv[:, c], ring[:, (KD + 2 * CT + 1 + c) % 4], ACT.Abs,
                                         bias=bdt[:, c:c + 1]).then_inc(act_read, 1)
                act.wait_ge(act_read, seen + KD + 3 * CT)
                nc.scalar.activation(du[:], cv[:], ACT.Exp, scale=-1.0).then_inc(exp_done, 1)
                act.wait_ge(one_added, b + 1)
                nc.scalar.activation(cv[:], ew[:], ACT.Ln).then_inc(ln_done, 1)
                act.wait_ge(dt_ready, b + 1)

                def decay(n, i):
                    act.wait_ge(bank_full, full + (KD + 3 * CT + 1) + 2 * n + 1)
                    act.wait_ge(dbx_ready, b * NS + n + 1)
                    nc.scalar.activation(bsb[:, i], ring[:, i], ACT.Copy).then_inc(act_read, 1)
                    act.wait_ge(h_scanned, b * NS + n + 1)
                    for c in range(CT):
                        e = nc.scalar.activation(dA[:, i, c, 1:S], dt[:, c, 1:S], ACT.Exp,
                                                 scale=a_neg[:, c, bass.ds(n, 1)])
                    e.then_inc(dA_ready, 1)

                with act.Fori(0, NS // 2) as pair:
                    decay(2 * pair, 0)
                    decay(2 * pair + 1, 1)

        @block.vector
        def _(dve):
            dve.wait_ge(a_set, 1)
            nc.vector.tensor_scalar(a_neg[:], a_neg[:], -1.0, None, ALU.mult).then_inc(a_set, 1)
            dve.wait_ge(w_loaded, 16 * 8)
            dve.wait_ge(consts_set, 3)
            for c in range(CT):
                last = nc.vector.tensor_scalar(diag_d[:, c], ident[:], dsk[:, c:c + 1], None, ALU.mult)
            last.then_inc(consts_set, 1)
            dve.sem_inc(dve_read, 2)
            dve.sem_inc(h_scanned, 2)
            DSTEP = DC - 1 + 2 + 2 + 4
            with dve.Fori(0, B) as b:
                steps = [0]

                def step(ins):
                    steps[0] += 1
                    ins.then_inc(dve_step, 1)
                    dve.wait_ge(dve_step, b * DSTEP + steps[0])

                read = b * DREAD + 2
                dve.wait_ge(act_read, b * AREAD + KD + CT)
                for j in range(DC):
                    for c in range(CT):
                        tap, w = xs_pad[:, c, j:j + S], cw[:, c, j:j + 1]
                        if j == 0:
                            ins = nc.vector.tensor_scalar(cv[:, c], tap, w, None, ALU.mult)
                        else:
                            ins = nc.vector.scalar_tensor_tensor(cv[:, c], tap, w, cv[:, c], ALU.mult, ALU.add)
                        if j == DC - 1:
                            ins.then_inc(conv_done, 1)
                    if j < DC - 1:
                        step(ins)
                dve.wait_ge(bank_full, b * RING + KD + 2 * CT + 1)
                xd = ring[:, (KD + 2 * CT) % 4]
                nc.vector.tensor_copy(xdf[:], xd).then_inc(xd_ready, 1)
                step(nc.vector.tensor_copy(xd3[:, 0], xd))
                nc.vector.tensor_tensor(xdr[:], xd, xd3[:, 0], ALU.subtract).then_inc(dve_read, 1)
                dve.wait_ge(dve_read, read + 1)
                step(nc.vector.tensor_copy(xd3[:, 1], xdr[:]))
                nc.vector.tensor_tensor(xd3[:, 2], xdr[:], xd3[:, 1], ALU.subtract).then_inc(xd_ready, 1)
                for c in range(CT):
                    dve.wait_ge(act_read, b * AREAD + KD + 2 * CT + c + 1)
                    nc.vector.tensor_scalar(relu_dt[:, c], ring[:, (KD + 2 * CT + 1 + c) % 4], bdt[:, c:c + 1], 0.0,
                                            ALU.add, ALU.max).then_inc(dve_read, 1)
                dve.wait_ge(exp_done, b + 1)
                nc.vector.tensor_scalar(ew[:], du[:], 1.0, None, ALU.add).then_inc(one_added, 1)
                dve.wait_ge(one_added, b + 1)
                dve.wait_ge(ln_done, b + 1)
                step(nc.vector.scalar_tensor_tensor(ew[:], ew[:], -1.0, du[:], ALU.add, ALU.subtract))
                step(nc.vector.tensor_tensor(ew[:], cv[:], ew[:], ALU.subtract))
                dve.wait_ge(dve_read, read + 1 + CT)
                nc.vector.tensor_tensor(dt[:], ew[:], relu_dt[:], ALU.add).then_inc(dt_ready, 1)
                dve.wait_ge(dt_ready, b + 1)
                nc.vector.tensor_tensor(du[:], dt[:], xs[:], ALU.mult).then_inc(du_ready, 1)

                def scan(n, i):
                    dve.wait_ge(dA_ready, b * NS + n + 1)
                    dve.wait_ge(dbx_ready, b * NS + n + 3)
                    dve.wait_ge(y_added, b * NS + n + 1)
                    nc.vector.tensor_tensor_scan(h[:, i].rearrange("p c s -> p (c s)"),
                                                 dA[:, i].rearrange("p c s -> p (c s)"),
                                                 dbx[:, i].rearrange("p c s -> p (c s)"),
                                                 0.0, ALU.mult, ALU.add).then_inc(h_scanned, 1)
                    dve.wait_ge(h_scanned, b * NS + n + 3)
                    dve.wait_ge(bank_full, b * RING + (KD + 3 * CT + 1) + 2 * n + 2)
                    nc.vector.tensor_tensor(h[:, i], h[:, i], ring[:, 2 + i:3 + i].to_broadcast([P, CT, S]),
                                            ALU.mult).then_inc(dve_read, 1)

                with dve.Fori(0, NS // 2) as pair:
                    scan(2 * pair, 0)
                    scan(2 * pair + 1, 1)
                dve.wait_ge(y_added, (b + 1) * NS + 2)
                for c in range(CT):
                    g = nc.vector.tensor_tensor(cv[:, c], ps_y[:, c], zs[:, c], ALU.mult)
                g.then_inc(g_ready, 1)
                dve.wait_ge(xres_loaded, (b + 1) * 16)
                for k in range(2):
                    dve.wait_ge(bank_full, (b + 1) * RING - 1 + k)
                    r = nc.vector.tensor_tensor(x_res[:, 2 * k:2 * k + 2], ring[:, k].rearrange("p (t d) -> p t d", d=DM),
                                                x_res[:, 2 * k:2 * k + 2], ALU.add)
                    if k == 0:
                        r.then_inc(dve_step, 1)
                        steps[0] += 1
                r.then_inc(dve_step, 1)
                steps[0] += 1
                dve.wait_ge(dve_step, b * DSTEP + steps[0])
                for t in range(TT):
                    s = nc.vector.bn_stats(stats[:, t], x_res[:, t])
                step(s)
                dve.sem_inc(stats_seen, 1)
                for t in range(TT):
                    s = nc.vector.bn_aggr(mv[:, t], stats[:, t])
                step(s)
                nc.vector.tensor_scalar(mv[:, :, 1], mv[:, :, 1], EPS, None, ALU.add).then_inc(var_ready, 1)
                dve.wait_ge(rstd_ready, b + 1)
                for t in range(TT):
                    o = nc.vector.tensor_scalar(x1[:, bass.ds(b * TT + t, 1), :].rearrange("p o d -> p (o d)"),
                                                x_res[:, t], mv[:, t, 0:1], rstd[:, t:t + 1], ALU.subtract, ALU.mult)
                    if t >= TT - 2:
                        o.then_inc(dve_read, 1)
                assert steps[0] == DSTEP, steps

        @block.tensor
        def _(pe):
            pe.sem_inc(x_in_free, 1)
            pe.sem_inc(y_added, 2)
            pe.wait_ge(w_loaded, 16 * 8)
            pe.wait_ge(consts_set, 4)

            def state_row(s, bank):
                for part in range(3):
                    mm = nc.tensor.matmul(ring[:, bank], sel[:, s, :] if isinstance(s, int) else
                                          sel[:, bass.ds(s, 1), :].rearrange("p o m -> p (o m)"),
                                          xd3[:, part], start=(part == 0), stop=(part == 2))
                mm.then_inc(bank_full, 1)

            with pe.Fori(0, B) as b:
                seen, read = b * AREAD, b * DREAD + 2
                pe.wait_ge(x_loaded, (b + 1) * 16)
                pe.wait_ge(dve_read, read)
                for k in range(KD):
                    for t in range(TT):
                        mm = nc.tensor.transpose(ring[:, k, t * P:(t + 1) * P], x_in[:, t, k * P:(k + 1) * P], ident[:])
                    mm.then_inc(bank_full, 1)
                for m in range(2 * CT):
                    i = KD + m
                    if m == 0:
                        pe.wait_ge(act_read, seen + KD)
                        pe.sem_inc(x_in_free, 1)
                    if i >= 4:
                        pe.wait_ge(act_read, seen + i - 3)
                    for k in range(KD):
                        mm = nc.tensor.matmul(ring[:, i % 4], win[:, k, m * P:(m + 1) * P], xt[:, k],
                                              start=(k == 0), stop=(k == KD - 1))
                    mm.then_inc(bank_full, 1)
                pe.wait_ge(xs_ready, (b + 1) * CT)
                pe.wait_ge(act_read, seen + KD + 2 * CT)
                i = KD + 2 * CT
                for c in range(CT):
                    mm = nc.tensor.matmul(ring[:, i % 4], wx[:, c], xs[:, c], start=(c == 0), stop=(c == CT - 1))
                mm.then_inc(bank_full, 1)
                pe.wait_ge(xd_ready, 2 * b + 1)
                for c in range(CT):
                    j = i + 1 + c
                    if j - 4 == i:
                        pe.wait_ge(dve_read, read + 1)
                    nc.tensor.matmul(ring[:, j % 4], wdt[:, c * P:(c + 1) * P], xdf[:],
                                     start=True, stop=True).then_inc(bank_full, 1)
                for c in range(CT):
                    nc.tensor.matmul(ps_y[:, c], diag_d[:, c], xs[:, c], start=True, stop=False, skip_group_check=True)
                pe.wait_ge(xd_ready, 2 * b + 2)
                pe.wait_ge(act_read, seen + KD + 3 * CT)
                pe.wait_ge(dve_read, read + 1 + CT)
                for n in range(2):
                    state_row(n, n)
                    state_row(NS + n, 2 + n)

                def add_state(n, i, more):
                    if more:
                        pe.wait_ge(act_read, seen + KD + 3 * CT + 1 + n)
                        state_row(n + 2, i)
                    pe.wait_ge(dve_read, read + 1 + CT + 1 + n)
                    for c in range(CT):
                        mm = nc.tensor.matmul(ps_y[:, c], ident[:], h[:, i, c], start=False, stop=not more,
                                              skip_group_check=True)
                    mm.then_inc(y_added, 1)
                    if more:
                        state_row(n + 2 + NS, 2 + i)

                with pe.Fori(0, NS // 2 - 1) as pair:
                    add_state(2 * pair, 0, True)
                    add_state(2 * pair + 1, 1, True)
                add_state(NS - 2, 0, False)
                add_state(NS - 1, 1, False)
                pe.wait_ge(g_ready, b + 1)
                for k in range(2):
                    for t in (2 * k, 2 * k + 1):
                        for c in range(CT):
                            mm = nc.tensor.matmul(ring[:, k, (t % 2) * DM:(t % 2 + 1) * DM],
                                                  cv[:, c, t * P:(t + 1) * P], wout[:, c],
                                                  start=(c == 0), stop=(c == CT - 1))
                    mm.then_inc(bank_full, 1)


H, DH, LC = 16, 64, 1601
HG = 4
NG = H // HG
GW = HG * DH
INNER = H * DH
KV = LC + S
KVP = KV + KV % 2
KT = -(-KV // P)
KL = KV - (KT - 1) * P
CTX_T = -(-LC // P)
CL = LC - (CTX_T - 1) * P
KC = [(c, min(512, KVP - c)) for c in range(0, KVP, 512)]
HALF = 512
SLOTS = (KT + 1) // 2
UNITS = 2 * HG
SCALE = 1.0 / DH ** 0.5

SCORES_AFTER = {(0, 0): -0.5, (0, 1): 1, (1, 0): 3, (1, 1): 4.5}
MAX_AFTER = {(0, 0): -1, (0, 1): 1, (1, 0): 3, (1, 1): 5}
EXP_AFTER = {(0, 0): 3, (0, 1): 3, (1, 0): 7, (1, 1): 8}
FOLD_AFTER = 3
Q_AFTER = 6
K_AFTER = [5, 6, 6, 8, 8]
LAG = 2


def attention(nc, ctx_rows, g1, b1, g2, b2, wq, wkv, wo, x1):
    PREP = [(2 * i, 2, P, 2 * i * P) for i in range(CTX_T // 2)] + [(CTX_T - 1, 1, CL, (CTX_T - 1) * P)]
    PREP += [(CTX_T, 2, P, LC), (CTX_T + 2, 1, P, LC + 2 * P), (CTX_T + 3, 1, P, LC + 3 * P)]
    VB = [(2 * i, 2) for i in range(SLOTS - 2)] + [(KT - 3, 1), (KT - 2, 1), (KT - 1, 1)]
    NPREP, NOUT = len(PREP), INNER // P
    NRING = HG + (HG // 2) * len(KC) + len(VB) + UNITS * (SLOTS + 1)
    NACT = HG + (HG // 2) * len(KC) + len(VB) + UNITS * SLOTS
    NSTART = 1 + len(KC) + len(VB)
    assert max(EXP_AFTER.values()) < SLOTS + 2 and HALF % (2 * P) == 0
    assert NSTART % 2 == 0 and len(KC) == len(K_AFTER) and min(K_AFTER) >= max(SCORES_AFTER.values())
    assert CTX_T % 2 == 1 and NPREP % 2 == NOUT % 2 == NRING % 2 == 0 and (UNITS * SLOTS) % 3 == 0
    RB = NPREP + NG * NRING + NOUT
    NT = CTX_T + TT
    V_AFTER = [min(i + LAG, SLOTS) for i in range(len(VB))]

    with ExitStack() as ctx:
        def sb(name, shape, dt=F32):
            return ctx.enter_context(nc.sbuf_tensor(name, shape, dt))

        def sem(name):
            return ctx.enter_context(nc.semaphore(name))

        ps_s = ctx.enter_context(nc.psum_tensor("a_scores", [P, 5 * 512], F32))
        ring = ctx.enter_context(nc.psum_tensor("a_ring", [P, 2, 512], F32))
        ps_o = ctx.enter_context(nc.psum_tensor("a_o", [P, 512], F32))

        kvh = sb("a_kvh", [P, KD, KVP], F32R)
        kvl = sb("a_kvl", [P, KD, KVP], F32R)
        probs = sb("a_probs", [P, 2, 2, KV])
        row_space, second = [probs[:, i].rearrange("p q k -> p (q k)") for i in range(2)]
        rows_all = row_space[:, 0:CTX_T * DM].rearrange("p (t d) -> p t d", d=DM)
        rows = [rows_all[:, t] for t in range(CTX_T)]
        lat = second[:, 0:TT * DM].rearrange("p (t d) -> p t d", d=DM)
        res = lat
        o_turned = second[:, TT * DM:TT * DM + 2 * S].rearrange("p (i s) -> p i s", s=S)
        keys = [sb(f"a_keys{i}", [P, KVP], F32R) for i in range(2)]
        vals = sb("a_vals", [P, KT, HG, 2 * DH], F32R)
        pth = sb("a_pth", [P, 3, 512], F32R)
        ptl = sb("a_ptl", [P, 3, 512], F32R)
        o_sb = sb("a_osb", [P, TT, INNER])
        wo_sb = sb("a_wo", [P, INNER // P, DM])
        w_raw = sb("a_wraw", [P, 3, KD, GW])
        wqh = sb("a_wqh", [P, KD, HG, 2, DH], F32R)
        wql = sb("a_wql", [P, KD, HG, 2, DH], F32R)
        wkh = sb("a_wkh", [P, KD, GW], F32R)
        wkl = sb("a_wkl", [P, KD, GW], F32R)
        wvh = sb("a_wvh", [P, KD, GW], F32R)
        wvl = sb("a_wvl", [P, KD, GW], F32R)
        qh = [sb(f"a_qh{i}", [P, S], F32R) for i in range(2)]
        ql = [sb(f"a_ql{i}", [P, S], F32R) for i in range(2)]
        turned = sb("a_turned", [P, 2, KD, 2 * P])
        ot = sb("a_ot", [P, 2 * P])
        gb = sb("a_gb", [P, 4, KD])
        ident = sb("a_ident", [P, P])
        fold = sb("a_fold", [P, DH])
        maxes = sb("a_maxes", [P, 2, 2])
        nmax = sb("a_nmax", [P, 2, 1])
        sums = sb("a_sums", [P, 2, 2, 2])
        total = sb("a_total", [P, 2, 2])
        rinv = sb("a_rinv", [P, 2, 2])
        stats = sb("a_stats", [P, NT, 6])
        mv = sb("a_mv", [P, NT, 2])
        rstd = sb("a_rstd", [P, NT])
        half = sb("a_half", [P, NT])

        consts_loaded = sem("a_consts_loaded")
        consts_set = sem("a_consts_set")
        rows_loaded = sem("a_rows_loaded")
        rows_free = sem("a_rows_free")
        w_loaded = sem("a_w_loaded")
        w_raw_free = sem("a_w_raw_free")
        w_high = sem("a_w_high")
        w_split = sem("a_w_split")
        w_free = sem("a_w_free")
        ring_full = sem("a_ring_full")
        ring_high = sem("a_ring_high")
        ring_free = sem("a_ring_free")
        turned_ready = sem("a_turned_ready")
        turned_high = sem("a_turned_high")
        scores1 = sem("a_scores1")
        scores2 = sem("a_scores2")
        max_done = sem("a_max_done")
        nmax_ready = sem("a_nmax_ready")
        exp1 = sem("a_exp1")
        exp2 = sem("a_exp2")
        pv_done = sem("a_pv_done")
        ot_done = sem("a_ot_done")
        total_done = sem("a_total_done")
        rinv_done = sem("a_rinv_done")
        var_ready = sem("a_var_ready")
        rstd_ready = sem("a_rstd_ready")
        rows_ready = sem("a_rows_ready")
        dve_step = sem("a_dve_step")
        waited = sem("a_waited")
        out_done = sem("a_out_done")

        block = ctx.enter_context(nc.Block())

        @block.sync
        def _(sp):
            for i, v in enumerate((g1, b1, g2, b2)):
                sp.dma_start(gb[:, i], v).then_inc(consts_loaded, 16)
            sp.dma_start(wo_sb[:], wo.rearrange("(i p) d -> p i d", p=P)).then_inc(consts_loaded, 16)
            q_src = wq.rearrange("(k p) n -> p k n", p=P)
            kv_src = wkv.rearrange("(k p) n -> p k n", p=P)
            with sp.Fori(0, B) as b:
                sp.wait_ge(rows_free, b + 1)
                src = ctx_rows[bass.ds(b, 1)].rearrange("o r d -> (o r) d")
                sp.dma_start(rows_all[:, 0:CTX_T - 1], src[0:(CTX_T - 1) * P].rearrange("(t p) d -> p t d", p=P)
                             ).then_inc(rows_loaded, 16)
                sp.dma_start(rows_all[0:CL, CTX_T - 1], src[(CTX_T - 1) * P:LC]).then_inc(rows_loaded, 16)
                with sp.Fori(0, NG) as g:
                    sp.wait_ge(w_raw_free, b * NG + g + 1)
                    sp.dma_start(w_raw[:, 0], q_src[:, :, bass.ds(g * GW, GW)]).then_inc(w_loaded, 16)
                    sp.dma_start(w_raw[:, 1], kv_src[:, :, bass.ds(g * GW, GW)]).then_inc(w_loaded, 16)
                    sp.dma_start(w_raw[:, 2], kv_src[:, :, bass.ds(g * GW + INNER, GW)]).then_inc(w_loaded, 16)

        @block.gpsimd
        def _(pool):
            nc.gpsimd.memset(ident[:], 0.0)
            nc.gpsimd.memset(fold[:], 0.0)
            nc.gpsimd.memset(mv[:], 1.0)
            nc.gpsimd.memset(kvh[:, :, KV:KVP].bitcast(F32), 0.0)
            nc.gpsimd.memset(kvl[:, :, KV:KVP].bitcast(F32), 0.0)
            nc.gpsimd.memset(half[:], -0.5).then_inc(consts_set, 1)
            pool.wait_ge(consts_set, 1)
            nc.gpsimd.affine_select(out=ident[:], in_=ident[:], compare_op=ALU.not_equal, fill=1.0, base=0,
                                    pattern=[[-1, P]], channel_multiplier=1)
            nc.gpsimd.affine_select(out=fold[:], in_=fold[:], compare_op=ALU.not_equal, fill=1.0, base=0,
                                    pattern=[[-1, DH]], channel_multiplier=1).then_inc(consts_set, 1)
            pool.wait_ge(consts_set, 2)
            nc.gpsimd.affine_select(out=fold[:], in_=fold[:], compare_op=ALU.not_equal, fill=1.0, base=-DH,
                                    pattern=[[-1, DH]], channel_multiplier=1).then_inc(consts_set, 1)
            pool.sem_inc(w_raw_free, 1)
            heads = w_raw[:, 0].rearrange("p k (h d) -> p k h d", d=DH)

            def split_weights(gi):
                pool.wait_ge(w_loaded, gi * 48 + 48)
                pool.wait_ge(w_free, gi + 1)
                pool.sem_inc(waited, 1)
                for r in range(2):
                    nc.gpsimd.tensor_copy(wqh[:, :, :, r], heads)
                nc.gpsimd.tensor_copy(wkh[:], w_raw[:, 1])
                nc.gpsimd.tensor_copy(wvh[:], w_raw[:, 2]).then_inc(w_high, 1)
                pool.wait_ge(w_high, gi + 1)
                for r in range(2):
                    nc.gpsimd.tensor_tensor(wql[:, :, :, r], heads, wqh[:, :, :, r].bitcast(F32), ALU.subtract)
                nc.gpsimd.tensor_tensor(wkl[:], w_raw[:, 1], wkh[:].bitcast(F32), ALU.subtract)
                nc.gpsimd.tensor_tensor(wvl[:], w_raw[:, 2], wvh[:].bitcast(F32), ALU.subtract).then_inc(w_split, 1)
                pool.wait_ge(w_split, gi + 1)
                pool.sem_inc(w_raw_free, 1)

            with pool.Fori(0, B) as b:
                pool.wait_ge(var_ready, 2 * b + 1)
                nc.gpsimd.tensor_tensor(rstd[:], mv[:, :, 1], half[:], ALU.pow).then_inc(rstd_ready, 1)
                with pool.Fori(0, NG) as g:
                    split_weights(b * NG + g)
                pool.wait_ge(var_ready, 2 * b + 2)
                nc.gpsimd.tensor_tensor(rstd[:, 0:TT], mv[:, 0:TT, 1], half[:, 0:TT], ALU.pow).then_inc(rstd_ready, 1)

        @block.scalar
        def _(act):
            act.wait_ge(consts_loaded, 16 * 5)
            act.sem_inc(exp1, 1)
            act.sem_inc(exp2, 1)
            act.sem_inc(ot_done, 1)
            with act.Fori(0, B) as b:
                for i, (t, n, r, col) in enumerate(PREP):
                    act.wait_ge(ring_full, b * RB + i + 1)
                    which = 0 if t < CTX_T else 2
                    for k in range(KD):
                        a = nc.scalar.activation(turned[:, i % 2, k, 0:n * r], ring[:, i % 2, k * 2 * P:k * 2 * P + n * r],
                                                 ACT.Identity, bias=gb[:, which + 1, k:k + 1], scale=gb[:, which, k:k + 1])
                    a.then_inc(turned_ready, 1)
                    act.wait_ge(turned_ready, b * NPREP + i + 1)
                    nc.scalar.activation(kvh[:, :, col:col + n * r], turned[:, i % 2, :, 0:n * r],
                                         ACT.Copy).then_inc(turned_high, 1)
                at, item, slot = [b * RB + NPREP, b * NG], [0], [0]

                def high(out):
                    act.wait_ge(ring_full, at[0] + item[0] + 1)
                    for o, part in out(item[0] % 2):
                        last = nc.scalar.activation(o, part, ACT.Copy)
                    last.then_inc(ring_high, 1)
                    item[0] += 1

                def high_q(hh):
                    high(lambda k: [(qh[hh % 2][:], ring[:, k])])

                def high_k(i):
                    c, n = KC[i]
                    high(lambda k: [(keys[0][0:DH, c:c + n], ring[0:DH, k, 0:n]),
                                    (keys[1][DH:P, c:c + n], ring[DH:P, k, 0:n])])

                def high_v(i):
                    t, n = VB[i]
                    r = KL if t == KT - 1 else P
                    high(lambda k: [(vals[0:r, t:t + n, :, 0:DH].rearrange("p t h d -> p (t h) d"),
                                     ring[0:r, k, 0:n * GW].rearrange("p (a d) -> p a d", d=DH))])

                def high_p(s):
                    act.wait_ge(pv_done, at[1] * UNITS * SLOTS + slot[0] + 1)
                    r, n = (KL, 256) if s == SLOTS - 1 else (P, 512)
                    high(lambda k: [(pth[0:r, slot[0] % 3, 0:n], ring[0:r, k, 0:n])])
                    slot[0] += 1

                def exp(u, q, part):
                    i = at[1] * UNITS * 2 + 2 * u + q
                    c0, c1 = (0, HALF) if part == 0 else (HALF, KV)
                    if part == 0:
                        act.wait_ge(nmax_ready, i + 1)
                    nc.scalar.activation(probs[:, u % 2, q, c0:c1], ps_s[:, c0:c1], ACT.Exp, bias=nmax[:, q],
                                         scale=SCALE, accum_out=sums[:, u % 2, q, part:part + 1]
                                         ).then_inc((exp1, exp2)[part], 1)

                def o_out(u):
                    act.wait_ge(pv_done, at[1] * UNITS * SLOTS + (u + 1) * SLOTS + 3)
                    nc.scalar.activation(ot[:], ps_o[:, 0:256], ACT.Copy).then_inc(ot_done, 1)

                high_q(0)
                for i in range(len(KC)):
                    high_k(i)
                high_v(0)
                exp(0, 0, 0)
                high_v(1)
                exp(0, 0, 1)
                high_v(2)
                high_v(3)
                high_v(4)
                exp(0, 1, 0)
                high_v(5)
                if EXP_AFTER[(1, 1)] < SLOTS:
                    exp(0, 1, 1)
                for i in range(6, len(VB)):
                    high_v(i)
                assert item[0] == NSTART

                def group(g, last):
                    at[:] = [b * RB + NPREP + NSTART + g * NRING, b * NG + g]
                    item[0] = slot[0] = 0
                    for u in range(UNITS):
                        more = u + 1 < UNITS or not last
                        if u > 0:
                            o_out(u - 1)
                        for s in range(SLOTS):
                            high_p(s)
                            if u > 0 and s == FOLD_AFTER:
                                item[0] += 1
                            for (q, part), after in EXP_AFTER.items():
                                if more and s == after:
                                    exp(u + 1, q, part)
                                if s == after - SLOTS:
                                    exp(u, q, part)
                            if u == 2 or (u == 6 and not last):
                                for i, after in enumerate(K_AFTER):
                                    if s == after:
                                        high_k(i)
                            if s == Q_AFTER and u % 2 == 0 and (u + 2 < UNITS or not last):
                                high_q(u // 2 + 1)
                            if u == UNITS - 1 and not last:
                                for i, after in enumerate(V_AFTER):
                                    if s == after:
                                        high_v(i)
                    o_out(UNITS - 1)
                    if not last:
                        for i, after in enumerate(V_AFTER):
                            if after == SLOTS:
                                high_v(i)

                with act.Fori(0, NG - 1) as g:
                    group(g, False)
                group(NG - 1, True)

        @block.vector
        def _(dve):
            dve.sem_inc(ring_free, 2)
            dve.wait_ge(consts_loaded, 16 * 5)
            dve.wait_ge(consts_set, 1)
            DSTEP = 2 + 3
            with dve.Fori(0, B) as b:
                steps = [0]

                def step(ins):
                    steps[0] += 1
                    ins.then_inc(dve_step, 1)
                    dve.wait_ge(dve_step, b * DSTEP + steps[0])

                dve.wait_ge(rows_loaded, (b + 1) * 32)
                for t in range(NT):
                    if t == CTX_T - 1:
                        s = nc.vector.bn_stats(stats[0:CL, t], rows[t][0:CL])
                    elif t < CTX_T:
                        s = nc.vector.bn_stats(stats[:, t], rows[t])
                    else:
                        s = nc.vector.bn_stats(stats[:, t], x1[:, bass.ds(b * TT + (t - CTX_T), 1)].rearrange("p o d -> p (o d)"))
                step(s)
                dve.sem_inc(waited, 1)
                for t in range(NT):
                    r = CL if t == CTX_T - 1 else P
                    s = nc.vector.bn_aggr(mv[0:r, t], stats[0:r, t])
                step(s)
                nc.vector.tensor_scalar(mv[:, :, 1], mv[:, :, 1], EPS, None, ALU.add).then_inc(var_ready, 1)
                dve.wait_ge(rstd_ready, 2 * b + 1)

                def normalised(i):
                    t, n, r, col = PREP[i]
                    for j in range(t, t + n):
                        if j < CTX_T:
                            src = dst = rows[j][0:r]
                        else:
                            src = x1[:, bass.ds(b * TT + (j - CTX_T), 1)].rearrange("p o d -> p (o d)")
                            dst = lat[:, j - CTX_T]
                        s = nc.vector.tensor_scalar(dst, src, mv[0:r, j, 0:1], rstd[0:r, j:j + 1],
                                                    ALU.subtract, ALU.mult)
                    s.then_inc(rows_ready, 1)

                def low_rows(i):
                    t, n, r, col = PREP[i]
                    dve.wait_ge(turned_high, b * NPREP + i + 1)
                    nc.vector.tensor_tensor(kvl[:, :, col:col + n * r], turned[:, i % 2, :, 0:n * r],
                                            kvh[:, :, col:col + n * r].bitcast(F32), ALU.subtract).then_inc(ring_free, 1)

                for i in range(3):
                    normalised(i)
                for i in range(NPREP):
                    low_rows(i)
                    if i + 3 < NPREP:
                        normalised(i + 3)

                at, item, highs, slot = [b * RB + NPREP, b * NG * NACT, b * NG], [0], [0], [0]

                def low(out):
                    dve.wait_ge(ring_high, at[1] + highs[0] + 1)
                    for o, part, hi in out(item[0] % 2):
                        last = nc.vector.tensor_tensor(o, part, hi.bitcast(F32), ALU.subtract)
                    last.then_inc(ring_free, 1)
                    item[0] += 1
                    highs[0] += 1

                def low_q(hh):
                    low(lambda k: [(ql[hh % 2][:], ring[:, k], qh[hh % 2][:])])

                def low_k(i):
                    c, n = KC[i]
                    low(lambda k: [(keys[0][DH:P, c:c + n], ring[0:DH, k, 0:n], keys[0][0:DH, c:c + n]),
                                   (keys[1][0:DH, c:c + n], ring[DH:P, k, 0:n], keys[1][DH:P, c:c + n])])

                def low_v(i):
                    t, n = VB[i]
                    r = KL if t == KT - 1 else P
                    low(lambda k: [(vals[0:r, t:t + n, :, DH:].rearrange("p t h d -> p (t h) d"),
                                    ring[0:r, k, 0:n * GW].rearrange("p (a d) -> p a d", d=DH),
                                    vals[0:r, t:t + n, :, 0:DH].rearrange("p t h d -> p (t h) d"))])

                def low_p(s):
                    r, n = (KL, 256) if s == SLOTS - 1 else (P, 512)
                    low(lambda k: [(ptl[0:r, slot[0] % 3, 0:n], ring[0:r, k, 0:n], pth[0:r, slot[0] % 3, 0:n])])
                    slot[0] += 1

                def row_max(u, q, part):
                    i = at[2] * UNITS * 2 + 2 * u + q
                    c0, c1 = (0, HALF) if part == 0 else (HALF, KV)
                    dve.wait_ge((scores1, scores2)[part], i + 1)
                    m = nc.vector.reduce_max(maxes[:, q, part:part + 1], ps_s[:, c0:c1], AX_X)
                    if part == 1:
                        m.then_inc(max_done, 1)
                        dve.wait_ge(max_done, i + 1)
                        nc.vector.tensor_scalar(nmax[:, q], maxes[:, q, 0:1], maxes[:, q, 1:2], -SCALE,
                                                ALU.max, ALU.mult).then_inc(nmax_ready, 1)

                def inverse(u):
                    dve.wait_ge(exp2, at[2] * UNITS * 2 + 2 * (u + 1) + 1)
                    nc.vector.tensor_tensor(total[:, u % 2], sums[:, u % 2, :, 0], sums[:, u % 2, :, 1],
                                            ALU.add).then_inc(total_done, 1)
                    dve.wait_ge(total_done, at[2] * UNITS + u + 1)
                    nc.vector.reciprocal(rinv[:, u % 2], total[:, u % 2]).then_inc(rinv_done, 1)

                def scaled_o(g, u):
                    dve.wait_ge(rinv_done, at[2] * UNITS + u + 1)
                    dve.wait_ge(ring_full, at[0] + item[0] + 1)
                    nc.vector.tensor_tensor(
                        o_sb[:, 2 * (u % 2):2 * (u % 2) + 2, bass.ds(g * GW + (u // 2) * DH, DH)],
                        ring[:, item[0] % 2, 0:2 * DH].rearrange("p (q d) -> p q d", d=DH),
                        rinv[:, u % 2].unsqueeze(2).to_broadcast([P, 2, DH]), ALU.mult).then_inc(ring_free, 1)
                    item[0] += 1

                low_q(0)
                for i in range(len(KC)):
                    low_k(i)
                row_max(0, 0, 0)
                row_max(0, 0, 1)
                for i in range(3):
                    low_v(i)
                row_max(0, 1, 0)
                low_v(3)
                low_v(4)
                row_max(0, 1, 1)
                for i in range(5, len(VB)):
                    low_v(i)

                def group(g, last):
                    at[:] = [b * RB + NPREP + NSTART + g * NRING, b * NG * NACT + NSTART + g * NACT, b * NG + g]
                    item[0] = highs[0] = slot[0] = 0
                    for u in range(UNITS):
                        more = u + 1 < UNITS or not last
                        for s in range(-1, SLOTS):
                            if s >= 0:
                                low_p(s)
                            if s == 2:
                                inverse(u)
                            if u > 0 and s == FOLD_AFTER:
                                scaled_o(g, u - 1)
                            for (q, part), after in MAX_AFTER.items():
                                if more and s == after:
                                    row_max(u + 1, q, part)
                            if u == 2 or (u == 6 and not last):
                                for i, after in enumerate(K_AFTER):
                                    if s == after:
                                        low_k(i)
                            if s == Q_AFTER and u % 2 == 0 and (u + 2 < UNITS or not last):
                                low_q(u // 2 + 1)
                            if u == UNITS - 1 and not last:
                                for i, after in enumerate(V_AFTER):
                                    if s == after:
                                        low_v(i)
                    if not last:
                        for i, after in enumerate(V_AFTER):
                            if after == SLOTS:
                                low_v(i)
                    scaled_o(g, UNITS - 1)
                    assert item[0] == NRING - last * NSTART and highs[0] == NACT - last * NSTART

                with dve.Fori(0, NG - 1) as g:
                    group(g, False)
                group(NG - 1, True)

                for i in range(NOUT):
                    dve.wait_ge(ring_full, b * RB + NPREP + NG * NRING + i + 1)
                    nc.vector.tensor_copy(o_turned[:, i % 2], ring[:, i % 2]).then_inc(ring_free, 1)
                dve.wait_ge(out_done, b + 1)
                for t in range(TT):
                    s = nc.vector.tensor_tensor(res[:, t], ps_s[:, t * 512:t * 512 + DM],
                                                x1[:, bass.ds(b * TT + t, 1)].rearrange("p o d -> p (o d)"), ALU.add)
                step(s)
                for t in range(TT):
                    s = nc.vector.bn_stats(stats[:, t], res[:, t])
                step(s)
                dve.sem_inc(waited, 1)
                for t in range(TT):
                    s = nc.vector.bn_aggr(mv[:, t], stats[:, t])
                step(s)
                nc.vector.tensor_scalar(mv[:, 0:TT, 1], mv[:, 0:TT, 1], EPS, None, ALU.add).then_inc(var_ready, 1)
                dve.wait_ge(rstd_ready, 2 * b + 2)
                for t in range(TT):
                    nc.vector.tensor_scalar(x1[:, bass.ds(b * TT + t, 1)].rearrange("p o d -> p (o d)"), res[:, t],
                                            mv[:, t, 0:1], rstd[:, t:t + 1], ALU.subtract, ALU.mult)
                assert steps[0] == DSTEP, steps

        @block.tensor
        def _(pe):
            pe.sem_inc(rows_free, 1)
            pe.sem_inc(w_free, 1)
            pe.sem_inc(pv_done, 3)
            pe.wait_ge(consts_loaded, 16 * 5)
            pe.wait_ge(consts_set, 3)
            with pe.Fori(0, B) as b:
                for i, (t, n, r, col) in enumerate(PREP):
                    pe.wait_ge(rows_ready, b * NPREP + i + 1)
                    pe.wait_ge(ring_free, b * RB + i + 1)
                    for k in range(KD):
                        for j in range(n):
                            src = rows[t + j][0:r] if t < CTX_T else lat[:, t + j - CTX_T]
                            o = k * 2 * P + j * r
                            mm = nc.tensor.transpose(ring[:, i % 2, o:o + r], src[:, k * P:(k + 1) * P], ident[0:r, 0:r])
                    mm.then_inc(ring_full, 1)
                pe.wait_ge(ring_free, b * RB + NPREP + 2)
                pe.sem_inc(waited, 1)
                at, item, slot = [b * RB + NPREP, b * NG], [0], [0]

                def bank():
                    pe.wait_ge(ring_free, at[0] + item[0] + 1)
                    item[0] += 1
                    return (item[0] - 1) % 2

                def product(out, lh, ll, rh, rl):
                    terms = [(x, y, k) for x, y in ((lh, rh), (lh, rl), (ll, rh)) for k in range(KD)]
                    for j, (x, y, k) in enumerate(terms):
                        mm = nc.tensor.matmul(out, x(k), y(k), start=(j == 0), stop=(j == len(terms) - 1))
                    return mm

                def make_q(hh):
                    hh %= HG
                    k0 = bank()
                    product(ring[:, k0], *[lambda k, w=w: w[:, k, hh].rearrange("p r d -> p (r d)") for w in (wqh, wql)],
                            *[lambda k, w=w: w[:, k, LC:KV] for w in (kvh, kvl)]).then_inc(ring_full, 1)

                def make_k(pair, i):
                    c, n = KC[i]
                    k0 = bank()
                    product(ring[:, k0, 0:n], *[lambda k, w=w: w[:, k, pair * P:(pair + 1) * P] for w in (wkh, wkl)],
                            *[lambda k, w=w: w[:, k, c:c + n] for w in (kvh, kvl)]).then_inc(ring_full, 1)

                def make_v(i):
                    t, n = VB[i]
                    r = KL if t == KT - 1 else P
                    k0 = bank()
                    for j in range(n):
                        c = (t + j) * P
                        mm = product(ring[0:r, k0, j * GW:(j + 1) * GW],
                                     *[lambda k, w=w: w[:, k, c:c + r] for w in (kvh, kvl)],
                                     *[lambda k, w=w: w[:, k] for w in (wvh, wvl)])
                    mm.then_inc(ring_full, 1)

                def scores(u, q, part):
                    hh, t = u // 2, 2 * (u % 2) + q
                    pe.wait_ge((exp1, exp2)[part], at[1] * UNITS * 2 + 2 * u + q + 1)
                    for c, n in (KC[:HALF // 512] if part == 0 else KC[HALF // 512:]):
                        for j, w in enumerate((qh, ql)):
                            mm = nc.tensor.matmul(ps_s[:, c:c + n], w[hh % 2][:, t * P:(t + 1) * P],
                                                  keys[hh % 2][:, c:c + n], start=(j == 0), stop=(j == 1))
                    mm.then_inc((scores1, scores2)[part], 1)

                def turn_p(u, s):
                    if s in (0, HALF // (2 * P)):
                        pe.wait_ge(exp1 if s == 0 else exp2, at[1] * UNITS * 2 + 2 * (u + 1) + 1)
                    k0 = bank()
                    for j in range(1 if s == SLOTS - 1 else 2):
                        c = (2 * s + j) * P
                        r = min(P, KV - c)
                        for q in range(2):
                            mm = nc.tensor.transpose(ring[0:r, k0, j * 256 + q * P:j * 256 + (q + 1) * P],
                                                     probs[:, u % 2, q, c:c + r], ident[:])
                    mm.then_inc(ring_full, 1)
                    return item[0]

                def add_o(u, s, ready):
                    if s == 0:
                        pe.wait_ge(ot_done, at[1] * UNITS + u + 1)
                    pe.wait_ge(ring_free, at[0] + ready + 2)
                    i = slot[0] % 3
                    for j in range(1 if s == SLOTS - 1 else 2):
                        t = 2 * s + j
                        r = min(P, KV - t * P)
                        for w in (pth, ptl):
                            mm = nc.tensor.matmul(ps_o[:, 0:256], vals[0:r, t, u // 2], w[0:r, i, j * 256:(j + 1) * 256],
                                                  start=(t == 0 and w is pth), stop=(t == KT - 1 and w is ptl))
                    mm.then_inc(pv_done, 1)
                    slot[0] += 1

                def fold_o(u):
                    pe.wait_ge(ot_done, at[1] * UNITS + u + 2)
                    k0 = bank()
                    for q in range(2):
                        mm = nc.tensor.matmul(ring[:, k0, q * DH:(q + 1) * DH], ot[:, q * P:(q + 1) * P], fold[:],
                                              start=True, stop=True)
                    mm.then_inc(ring_full, 1)

                pe.wait_ge(w_split, b * NG + 1)
                make_q(0)
                for i in range(len(KC)):
                    make_k(0, i)
                pe.wait_ge(ring_free, at[0] + item[0] + 2)
                scores(0, 0, 0)
                scores(0, 0, 1)
                for i in range(3):
                    make_v(i)
                scores(0, 1, 0)
                make_v(3)
                make_v(4)
                scores(0, 1, 1)
                for i in range(5, len(VB)):
                    make_v(i)

                def next_scores(u, s, more, last, needs):
                    for (q, part), after in SCORES_AFTER.items():
                        if more and s == after:
                            if (q, part) == (0, 0):
                                if needs > 0:
                                    pe.wait_ge(ring_free, at[0] + needs + 2)
                                if u + 1 == UNITS - 2:
                                    pe.sem_inc(w_free, 1)
                            scores(u + 1, q, part)

                def group(g, last):
                    at[:] = [b * RB + NPREP + NSTART + g * NRING, b * NG + g]
                    item[0] = slot[0] = needs = 0
                    for u in range(UNITS):
                        more = u + 1 < UNITS or not last
                        ready = {}
                        for s in range(-1, SLOTS):
                            if s >= 0:
                                ready[s] = turn_p(u, s)
                                next_scores(u, s - 0.5, more, last, needs)
                            if s >= LAG:
                                add_o(u, s - LAG, ready[s - LAG])
                            if u > 0 and s == FOLD_AFTER:
                                fold_o(u - 1)
                            next_scores(u, s, more, last, needs)
                            if u == 2 or (u == 6 and not last):
                                for i, after in enumerate(K_AFTER):
                                    if s == after:
                                        if u == 6 and i == 0:
                                            pe.wait_ge(w_split, at[1] + 2)
                                        make_k((u + 2) // 4 % 2, i)
                                        needs = item[0]
                            if s == Q_AFTER and u % 2 == 0 and (u + 2 < UNITS or not last):
                                make_q(u // 2 + 1)
                                needs = item[0] if u != 2 and u != 6 else needs
                            if u == UNITS - 1 and not last:
                                for i, after in enumerate(V_AFTER):
                                    if s == after:
                                        make_v(i)
                        for s in range(SLOTS - LAG, SLOTS):
                            add_o(u, s, ready[s])
                        if last and u == UNITS - 2:
                            pe.sem_inc(rows_free, 1)
                    if not last:
                        for i, after in enumerate(V_AFTER):
                            if after == SLOTS:
                                make_v(i)
                    fold_o(UNITS - 1)
                    assert item[0] == NRING - last * NSTART

                with pe.Fori(0, NG - 1) as g:
                    group(g, False)
                group(NG - 1, True)

                base = b * RB + NPREP + NG * NRING
                pe.wait_ge(ring_free, base + 2)
                for i in range(NOUT + 1):
                    if i < NOUT:
                        pe.wait_ge(ring_free, base + i + 1)
                        for t in range(TT):
                            mm = nc.tensor.transpose(ring[:, i % 2, t * P:(t + 1) * P], o_sb[:, t, i * P:(i + 1) * P], ident[:])
                        mm.then_inc(ring_full, 1)
                    if i > 0:
                        pe.wait_ge(ring_free, base + i + 2)
                        for t in range(TT):
                            mm = nc.tensor.matmul(ps_s[:, t * 512:t * 512 + DM], o_turned[:, (i - 1) % 2, t * P:(t + 1) * P],
                                                  wo_sb[:, i - 1], start=(i == 1), stop=(i == NOUT))
                mm.then_inc(out_done, 1)


E, NSH, TOPK, HID = 8, 2, 2, 512
EX = E + NSH
MT = HID // P
NTILE = B * TT
O0 = B * TT + 1


def experts(nc, router_t, expert_bias, w1_t, w3_t, w2_t, x2, out):
    with ExitStack() as ctx:
        def sb(name, shape, dt=F32):
            return ctx.enter_context(nc.sbuf_tensor(name, shape, dt))

        def sem(name):
            return ctx.enter_context(nc.semaphore(name))

        ps_h = ctx.enter_context(nc.psum_tensor("e_h", [P, 2, 2, 512], F32))
        ps_o = ctx.enter_context(nc.psum_tensor("e_o", [P, TT, 512], F32))

        xth = sb("e_xth", [P, KD, B * S], F32R)
        xtl = sb("e_xtl", [P, KD, B * S], F32R)
        xt = sb("e_xt", [P, 2, KD, S])
        router = sb("e_router", [P, KD, E])
        bias = sb("e_bias", [P, E])
        ident = sb("e_ident", [P, P])
        w_raw = [sb(f"e_raw{i}", [P, 1024]) for i in range(3)]
        wh = [[sb(f"e_wh{i}{j}", [P, 1024], F32R) for j in range(3)] for i in range(2)]
        wl = [[sb(f"e_wl{i}{j}", [P, 1024], F32R) for j in range(3)] for i in range(2)]
        silu = sb("e_silu", [P, 2, S])
        gate = sb("e_gate", [P, 2, S])
        gh = sb("e_gh", [P, MT, S], F32R)
        gl = sb("e_gl", [P, MT, S], F32R)
        logits = sb("e_logits", [P, NTILE, E])
        above = sb("e_above", [P, NTILE, E, E])
        equal = sb("e_equal", [P, NTILE, E, E])
        lower = sb("e_lower", [P, E, E])
        rank = sb("e_rank", [P, NTILE, E])
        top = sb("e_top", [P, NTILE])
        share = sb("e_share", [P, NTILE, E])
        whole = sb("e_whole", [P, NTILE])
        combine = sb("e_combine", [P, NTILE, EX])
        stats = sb("e_stats", [P, NTILE, 6])
        mv = sb("e_mv", [P, NTILE, 2])
        rstd = sb("e_rstd", [P, NTILE])
        half = sb("e_half", [P, NTILE])
        x3 = sb("e_x3", [P, NTILE, DM])

        consts_loaded = sem("e_consts_loaded")
        consts_set = sem("e_consts_set")
        w_loaded = sem("e_w_loaded")
        w_raw_free = sem("e_w_raw_free")
        w_high = sem("e_w_high")
        w_split = sem("e_w_split")
        rows_turned = sem("e_rows_turned")
        xt_high = sem("e_xt_high")
        xt_low = sem("e_xt_low")
        logits_done = sem("e_logits_done")
        logits_read = sem("e_logits_read")
        dve_step = sem("e_dve_step")
        shifted = sem("e_shifted")
        exp_done = sem("e_exp_done")
        h_done = sem("e_h_done")
        silu_done = sem("e_silu_done")
        gate_done = sem("e_gate_done")
        g_high = sem("e_g_high")
        g_low = sem("e_g_low")
        o_done = sem("e_o_done")
        o_read = sem("e_o_read")
        var_ready = sem("e_var_ready")
        rstd_ready = sem("e_rstd_ready")
        x3_ready = sem("e_x3_ready")
        stored = sem("e_stored")
        waited = sem("e_waited")

        block = ctx.enter_context(nc.Block())

        @block.sync
        def _(sp):
            sp.dma_start(router[:], router_t.rearrange("(k p) e -> p k e", p=P)).then_inc(consts_loaded, 16)
            sp.dma_start(bias[:], expert_bias.partition_broadcast(P)).then_inc(consts_loaded, 16)
            with sp.Fori(0, EX) as e:
                sp.wait_ge(w_raw_free, e + 1)
                for raw, w, n in zip(w_raw, (w1_t, w3_t, w2_t), (HID, HID, DM)):
                    sp.dma_start(raw[:].rearrange("p (k n) -> p k n", n=n),
                                 w[bass.ds(e, 1)].rearrange("o (k p) n -> p (o k) n", p=P)).then_inc(w_loaded, 16)
            for b in range(B):
                sp.wait_ge(x3_ready, b + 1)
                sp.dma_start(out[b].rearrange("(t p) d -> p t d", p=P), x3[:, b * TT:(b + 1) * TT]).then_inc(stored, 16)
            sp.wait_ge(stored, 16 * B)

        @block.gpsimd
        def _(pool):
            nc.gpsimd.memset(ident[:], 0.0)
            nc.gpsimd.memset(lower[:], 1.0)
            nc.gpsimd.memset(combine[:, :, E:], 1.0)
            nc.gpsimd.memset(half[:], -0.5).then_inc(consts_set, 1)
            pool.wait_ge(consts_set, 1)
            nc.gpsimd.affine_select(out=ident[:], in_=ident[:], compare_op=ALU.not_equal, fill=1.0, base=0,
                                    pattern=[[-1, P]], channel_multiplier=1)
            nc.gpsimd.affine_select(out=lower[:], in_=lower[:], compare_op=ALU.is_gt, fill=0.0, base=0,
                                    pattern=[[1, E], [-1, E]], channel_multiplier=0).then_inc(consts_set, 1)
            pool.sem_inc(w_raw_free, 1)
            with pool.Fori(0, EX // 2) as pair:
                for i in range(2):
                    e = 2 * pair + i
                    pool.wait_ge(w_loaded, e * 48 + 48)
                    pool.wait_ge(o_done, (e - 1) * B * TT + O0)
                    pool.sem_inc(waited, 1)
                    for j in range(3):
                        hi = nc.gpsimd.tensor_copy(wh[i][j][:], w_raw[j][:])
                    hi.then_inc(w_high, 1)
                    pool.wait_ge(w_high, e + 1)
                    for j in range(3):
                        lo = nc.gpsimd.tensor_tensor(wl[i][j][:], w_raw[j][:], wh[i][j][:].bitcast(F32), ALU.subtract)
                    lo.then_inc(w_split, 1)
                    pool.wait_ge(w_split, e + 1)
                    pool.sem_inc(w_raw_free, 1)
            pool.wait_ge(var_ready, 1)
            nc.gpsimd.tensor_tensor(rstd[:], mv[:, :, 1], half[:], ALU.pow).then_inc(rstd_ready, 1)

        @block.scalar
        def _(act):
            act.sem_inc(silu_done, 2)
            for i in range(B * KD):
                b, k = divmod(i, KD)
                act.wait_ge(rows_turned, i + 1)
                nc.scalar.activation(xth[:, k, b * S:(b + 1) * S], ps_h[:, i // 2 % 2, i % 2], ACT.Copy).then_inc(xt_high, 1)
            act.wait_ge(shifted, 1)
            nc.scalar.activation(share[:], share[:], ACT.Exp).then_inc(exp_done, 1)
            with act.Fori(0, EX) as e:
                with act.Fori(0, B) as b:
                    n = e * B + b
                    for m in range(MT + 1):
                        if m < MT:
                            act.wait_ge(h_done, n * MT + m + 1)
                            act.wait_ge(gate_done, n * MT + m + 1)
                            nc.scalar.activation(silu[:, m % 2], ps_h[:, m % 2, 0], ACT.Silu).then_inc(silu_done, 1)
                        if m > 0:
                            act.wait_ge(gate_done, n * MT + m - 1 + 3)
                            act.wait_ge(o_done, n * TT + O0)
                            nc.scalar.activation(gh[:, m - 1], gate[:, (m - 1) % 2], ACT.Copy).then_inc(g_high, 1)

        @block.vector
        def _(dve):
            def read_logits(b):
                dve.wait_ge(logits_done, b + 1)
                nc.vector.tensor_tensor(logits[:, b * TT:(b + 1) * TT], ps_o[:, :, 0:E],
                                        bias[:].unsqueeze(1).to_broadcast([P, TT, E]), ALU.add).then_inc(logits_read, 1)

            dve.sem_inc(gate_done, 2)
            dve.sem_inc(g_low, 2)
            dve.sem_inc(o_read, TT)
            dve.wait_ge(consts_loaded, 32)
            for i in range(B * KD):
                b, k = divmod(i, KD)
                cols = slice(b * S, (b + 1) * S)
                src = ps_h[:, i // 2 % 2, i % 2]
                dve.wait_ge(xt_high, i + 1)
                if b >= 2:
                    dve.wait_ge(logits_done, b - 1)
                nc.vector.tensor_copy(xt[:, b % 2, k], src)
                nc.vector.tensor_tensor(xtl[:, k, cols], src, xth[:, k, cols].bitcast(F32), ALU.subtract).then_inc(xt_low, 1)
                if k == KD - 1 and b > 0:
                    read_logits(b - 1)
            read_logits(B - 1)
            steps = [0]

            def step(ins):
                steps[0] += 1
                ins.then_inc(dve_step, 1)
                dve.wait_ge(dve_step, steps[0])

            dve.wait_ge(consts_set, 2)
            dve.wait_ge(logits_read, B)
            other = logits[:].unsqueeze(2).to_broadcast([P, NTILE, E, E])
            own = logits[:].unsqueeze(3).to_broadcast([P, NTILE, E, E])
            nc.vector.tensor_tensor(above[:], other, own, ALU.is_gt)
            nc.vector.reduce_max(top[:], logits[:], AX_X)
            step(nc.vector.tensor_tensor(equal[:], other, own, ALU.is_equal))
            nc.vector.tensor_tensor(share[:], logits[:], top[:].unsqueeze(2).to_broadcast([P, NTILE, E]),
                                    ALU.subtract).then_inc(shifted, 1)
            flat = lambda t: t.rearrange("p t e j -> p t (e j)")
            step(nc.vector.tensor_tensor(flat(equal[:]), flat(equal[:]),
                                         lower[:].rearrange("p e j -> p (e j)").unsqueeze(1).to_broadcast([P, NTILE, E * E]),
                                         ALU.mult))
            step(nc.vector.tensor_tensor(above[:], above[:], equal[:], ALU.add))
            step(nc.vector.reduce_sum(rank[:], above[:], AX_X))
            dve.wait_ge(exp_done, 1)
            step(nc.vector.scalar_tensor_tensor(share[:], rank[:], float(TOPK), share[:], ALU.is_lt, ALU.mult))
            step(nc.vector.reduce_sum(whole[:], share[:], AX_X))
            step(nc.vector.reciprocal(whole[:], whole[:]))
            step(nc.vector.tensor_tensor(combine[:, :, 0:E], share[:], whole[:].unsqueeze(2).to_broadcast([P, NTILE, E]),
                                         ALU.mult))

            with dve.Fori(0, EX) as e:
                with dve.Fori(0, B) as b:
                    n = e * B + b
                    for m in range(MT + 1):
                        if m < MT:
                            dve.wait_ge(silu_done, n * MT + m + 3)
                            dve.wait_ge(g_low, n * MT + m + 1)
                            nc.vector.tensor_tensor(gate[:, m % 2], silu[:, m % 2], ps_h[:, m % 2, 1],
                                                    ALU.mult).then_inc(gate_done, 1)
                        if m > 0:
                            dve.wait_ge(g_high, n * MT + m)
                            nc.vector.tensor_tensor(gl[:, m - 1], gate[:, (m - 1) % 2], gh[:, m - 1].bitcast(F32),
                                                    ALU.subtract).then_inc(g_low, 1)
                    for t in range(TT):
                        dve.wait_ge(o_done, n * TT + t + 1 + O0)
                        row = x2[:, bass.ds(b * TT + t, 1)].rearrange("p o d -> p (o d)")
                        w = combine[:, bass.ds(b * TT + t, 1), bass.ds(e, 1)].rearrange("p o e -> p (o e)")
                        nc.vector.scalar_tensor_tensor(row, ps_o[:, t, 0:DM], w, row, ALU.mult, ALU.add).then_inc(o_read, 1)
            dve.wait_ge(o_read, EX * B * TT + TT)
            for t in range(NTILE):
                s = nc.vector.bn_stats(stats[:, t], x2[:, t])
            step(s)
            for t in range(NTILE):
                s = nc.vector.bn_aggr(mv[:, t], stats[:, t])
            step(s)
            nc.vector.tensor_scalar(mv[:, :, 1], mv[:, :, 1], EPS, None, ALU.add).then_inc(var_ready, 1)
            dve.wait_ge(rstd_ready, 1)
            for t in range(NTILE):
                s = nc.vector.tensor_scalar(x3[:, t], x2[:, t], mv[:, t, 0:1], rstd[:, t:t + 1], ALU.subtract, ALU.mult)
                if t % TT == TT - 1:
                    s.then_inc(x3_ready, 1)

        @block.tensor
        def _(pe):
            pe.sem_inc(o_done, O0)
            pe.wait_ge(consts_set, 2)
            pe.wait_ge(consts_loaded, 32)

            def route(b):
                pe.wait_ge(xt_low, (b + 1) * KD)
                if b > 0:
                    pe.wait_ge(logits_read, b)
                for t in range(TT):
                    for k in range(KD):
                        mm = nc.tensor.matmul(ps_o[:, t, 0:E], xt[:, b % 2, k, t * P:(t + 1) * P], router[:, k],
                                              start=(k == 0), stop=(k == KD - 1))
                mm.then_inc(logits_done, 1)

            for i in range(B * KD):
                b, k = divmod(i, KD)
                if i >= 4:
                    pe.wait_ge(xt_low, i - 3)
                for t in range(TT):
                    mm = nc.tensor.transpose(ps_h[:, i // 2 % 2, i % 2, t * P:(t + 1) * P],
                                             x2[:, b * TT + t, k * P:(k + 1) * P], ident[:])
                mm.then_inc(rows_turned, 1)
                if k == KD - 1 and b > 0:
                    route(b - 1)
            route(B - 1)
            pe.wait_ge(xt_low, B * KD)

            with pe.Fori(0, EX // 2) as pair:
                for i in range(2):
                    e = 2 * pair + i
                    pe.wait_ge(w_split, e + 1)
                    pe.sem_inc(waited, 1)
                    w1h, w3h = [wh[i][j][:].rearrange("p (k n) -> p k n", n=HID) for j in range(2)]
                    w1l, w3l = [wl[i][j][:].rearrange("p (k n) -> p k n", n=HID) for j in range(2)]
                    w2h, w2l = [w[i][2][:].rearrange("p (k n) -> p k n", n=DM) for w in (wh, wl)]
                    with pe.Fori(0, B) as b:
                        n = e * B + b

                        def hidden(m):
                            for part, (h, l) in enumerate(((w1h, w1l), (w3h, w3l))):
                                pe.wait_ge((silu_done, gate_done)[part], n * MT + m + 1)
                                terms = [(x, y, k) for x, y in ((h, xth), (h, xtl), (l, xth)) for k in range(KD)]
                                for j, (x, y, k) in enumerate(terms):
                                    mm = nc.tensor.matmul(ps_h[:, m % 2, part], x[:, k, m * P:(m + 1) * P],
                                                          y[:, k, bass.ds(b * S, S)], start=(j == 0), stop=(j == len(terms) - 1))
                            mm.then_inc(h_done, 1)

                        def down(m):
                            pe.wait_ge(g_low, n * MT + m + 3)
                            for t in range(TT):
                                if m == 0:
                                    pe.wait_ge(o_read, n * TT + t + 1)
                                for j, (x, y) in enumerate(((gh, w2h), (gh, w2l), (gl, w2h))):
                                    mm = nc.tensor.matmul(ps_o[:, t, 0:DM], x[:, m, t * P:(t + 1) * P], y[:, m],
                                                          start=(m == 0 and j == 0), stop=(m == MT - 1 and j == 2))
                                if m == MT - 1:
                                    mm.then_inc(o_done, 1)

                        hidden(0)
                        hidden(1)
                        hidden(2)
                        down(0)
                        hidden(3)
                        for m in range(1, MT):
                            down(m)


def laid_out(x, ctx_1024, L0_attn_W_in, L0_attn_conv_w, L0_attn_conv_b, L0_attn_W_x, L0_attn_W_dt, L0_attn_b_dt,
             L0_attn_A_log, L0_attn_D, L0_attn_W_out, L0_xattn_g1, L0_xattn_b1, L0_xattn_g2, L0_xattn_b2, L0_xattn_Wq,
             L0_xattn_Wkv, L0_xattn_Wout, L0_ffn_router_w, L0_ffn_expert_bias, L0_ffn_w1, L0_ffn_w3, L0_ffn_w2,
             L0_ffn_sw1, L0_ffn_sw3, L0_ffn_sw2):
    import numpy as np
    a = np.asarray

    def columns(v):
        v = a(v)
        return v.reshape(-1, P, *v.shape[1:]).swapaxes(0, 1)

    def turned(w, shared):
        return np.concatenate([a(w), a(shared)]).transpose(0, 2, 1)

    arrays = {
        "x": a(x), "ctx": a(ctx_1024),
        "w_in_t": a(L0_attn_W_in).T, "conv_w": columns(a(L0_attn_conv_w).reshape(DI, DC)),
        "conv_b": columns(L0_attn_conv_b),
        "w_x_t": a(L0_attn_W_x).T, "w_dt_t": a(L0_attn_W_dt).T, "b_dt": columns(L0_attn_b_dt),
        "a_log": columns(L0_attn_A_log), "d_skip": columns(L0_attn_D), "w_out_t": a(L0_attn_W_out).T,
        "g1": columns(L0_xattn_g1), "b1": columns(L0_xattn_b1), "g2": columns(L0_xattn_g2), "b2": columns(L0_xattn_b2),
        "wq": a(L0_xattn_Wq), "wkv": a(L0_xattn_Wkv), "wo": a(L0_xattn_Wout),
        "router_t": a(L0_ffn_router_w).T, "expert_bias": a(L0_ffn_expert_bias),
        "w1_t": turned(L0_ffn_w1, L0_ffn_sw1), "w3_t": turned(L0_ffn_w3, L0_ffn_sw3),
        "w2_t": turned(L0_ffn_w2, L0_ffn_sw2),
    }
    return {name: np.ascontiguousarray(array) for name, array in arrays.items()}


def decoder(nc, t, out):
    with nc.sbuf_tensor("rows", [P, B * TT, DM], F32) as x:
        mamba(nc, t["x"], t["w_in_t"], t["conv_w"], t["conv_b"], t["w_x_t"], t["w_dt_t"], t["b_dt"], t["a_log"],
              t["d_skip"], t["w_out_t"], x)
        attention(nc, t["ctx"], t["g1"], t["b1"], t["g2"], t["b2"], t["wq"], t["wkv"], t["wo"], x)
        experts(nc, t["router_t"], t["expert_bias"], t["w1_t"], t["w3_t"], t["w2_t"], x, out)


def kernel(**inputs):
    from concourse import bacc
    from concourse.bass_utils import run_bass_kernel_spmd

    nc = bacc.Bacc("TRN2", target_bir_lowering=False, num_devices=1)
    arrays, handles = {}, {}
    for name, array in laid_out(**inputs).items():
        arrays[f"in_{name}_dram"] = array
        handles[name] = nc.dram_tensor(f"in_{name}_dram", array.shape, mybir.dt.from_np(array.dtype),
                                       kind="ExternalInput").ap()
    out = nc.dram_tensor("out_0_dram", (B, S, DM), F32, kind="ExternalOutput").ap()
    decoder(nc, handles, out)
    return run_bass_kernel_spmd(nc, [arrays], core_ids=[0]).results[0]["out_0_dram"]
```
